# Optimizing a Trainium2 kernel written in Bass

```python
import numpy as np
import jax
import jax.numpy as jnp

def _softmax(x, axis=-1):
    return jax.nn.softmax(x, axis=axis)

def _gelu(x):
    return jax.nn.gelu(x, approximate=True)

def _silu(x):
    return jax.nn.silu(x)

def _sigmoid(x):
    return jax.nn.sigmoid(x)

def _layernorm(x, axis=-1, eps=1e-05):
    m = jnp.mean(x, axis=axis, keepdims=True)
    v = jnp.var(x, axis=axis, keepdims=True)
    return (x - m) / jnp.sqrt(v + eps)

def _scatter_add(tgt, idx, src, axis=0):
    return tgt.at[idx].add(src)

def _segment_sum(src, seg, n):
    return jax.ops.segment_sum(src, seg, n)
kernel_name = 'mk_dlrm_tower_d1_rec_r8_072e66'

def setup_inputs(seed: int=0):
    np.random.seed(seed)
    _w = jnp.asarray

    def _rec_inputs():
        import jax
        import jax.numpy as jnp
        _tk = jax.random.key(seed)
        dense_ctx = jax.random.normal(jax.random.fold_in(_tk, 190), (1024, 16), jnp.float32)
        ids = jnp.stack([jax.random.randint(jax.random.fold_in(_tk, 200 + f), (1024,), 0, v, jnp.int32) for f, v in enumerate([125000, 12500, 1250, 1000, 1250, 125000, 12500, 1250, 1250, 1000, 1250, 12500, 125000, 1250, 12500, 12500, 12500, 1000, 1250, 1250, 1000, 1000, 1250, 1000, 12500, 125000, 1000, 12500, 1000, 1000, 1000, 12500])], axis=1)
        tbl_0 = 0.05 * jax.random.normal(jax.random.fold_in(_tk, 500 + 0), (125000, 16), jnp.float32)
        tbl_1 = 0.05 * jax.random.normal(jax.random.fold_in(_tk, 500 + 1), (12500, 16), jnp.float32)
        tbl_2 = 0.05 * jax.random.normal(jax.random.fold_in(_tk, 500 + 2), (1250, 16), jnp.float32)
        tbl_3 = 0.05 * jax.random.normal(jax.random.fold_in(_tk, 500 + 3), (1000, 16), jnp.float32)
        tbl_4 = 0.05 * jax.random.normal(jax.random.fold_in(_tk, 500 + 4), (1250, 16), jnp.float32)
        tbl_5 = 0.05 * jax.random.normal(jax.random.fold_in(_tk, 500 + 5), (125000, 16), jnp.float32)
        tbl_6 = 0.05 * jax.random.normal(jax.random.fold_in(_tk, 500 + 6), (12500, 16), jnp.float32)
        tbl_7 = 0.05 * jax.random.normal(jax.random.fold_in(_tk, 500 + 7), (1250, 16), jnp.float32)
        tbl_8 = 0.05 * jax.random.normal(jax.random.fold_in(_tk, 500 + 8), (1250, 16), jnp.float32)
        tbl_9 = 0.05 * jax.random.normal(jax.random.fold_in(_tk, 500 + 9), (1000, 16), jnp.float32)
        tbl_10 = 0.05 * jax.random.normal(jax.random.fold_in(_tk, 500 + 10), (1250, 16), jnp.float32)
        tbl_11 = 0.05 * jax.random.normal(jax.random.fold_in(_tk, 500 + 11), (12500, 16), jnp.float32)
        tbl_12 = 0.05 * jax.random.normal(jax.random.fold_in(_tk, 500 + 12), (125000, 16), jnp.float32)
        tbl_13 = 0.05 * jax.random.normal(jax.random.fold_in(_tk, 500 + 13), (1250, 16), jnp.float32)
        tbl_14 = 0.05 * jax.random.normal(jax.random.fold_in(_tk, 500 + 14), (12500, 16), jnp.float32)
        tbl_15 = 0.05 * jax.random.normal(jax.random.fold_in(_tk, 500 + 15), (12500, 16), jnp.float32)
        tbl_16 = 0.05 * jax.random.normal(jax.random.fold_in(_tk, 500 + 16), (12500, 16), jnp.float32)
        tbl_17 = 0.05 * jax.random.normal(jax.random.fold_in(_tk, 500 + 17), (1000, 16), jnp.float32)
        tbl_18 = 0.05 * jax.random.normal(jax.random.fold_in(_tk, 500 + 18), (1250, 16), jnp.float32)
        tbl_19 = 0.05 * jax.random.normal(jax.random.fold_in(_tk, 500 + 19), (1250, 16), jnp.float32)
        tbl_20 = 0.05 * jax.random.normal(jax.random.fold_in(_tk, 500 + 20), (1000, 16), jnp.float32)
        tbl_21 = 0.05 * jax.random.normal(jax.random.fold_in(_tk, 500 + 21), (1000, 16), jnp.float32)
        tbl_22 = 0.05 * jax.random.normal(jax.random.fold_in(_tk, 500 + 22), (1250, 16), jnp.float32)
        tbl_23 = 0.05 * jax.random.normal(jax.random.fold_in(_tk, 500 + 23), (1000, 16), jnp.float32)
        tbl_24 = 0.05 * jax.random.normal(jax.random.fold_in(_tk, 500 + 24), (12500, 16), jnp.float32)
        tbl_25 = 0.05 * jax.random.normal(jax.random.fold_in(_tk, 500 + 25), (125000, 16), jnp.float32)
        tbl_26 = 0.05 * jax.random.normal(jax.random.fold_in(_tk, 500 + 26), (1000, 16), jnp.float32)
        tbl_27 = 0.05 * jax.random.normal(jax.random.fold_in(_tk, 500 + 27), (12500, 16), jnp.float32)
        tbl_28 = 0.05 * jax.random.normal(jax.random.fold_in(_tk, 500 + 28), (1000, 16), jnp.float32)
        tbl_29 = 0.05 * jax.random.normal(jax.random.fold_in(_tk, 500 + 29), (1000, 16), jnp.float32)
        tbl_30 = 0.05 * jax.random.normal(jax.random.fold_in(_tk, 500 + 30), (1000, 16), jnp.float32)
        tbl_31 = 0.05 * jax.random.normal(jax.random.fold_in(_tk, 500 + 31), (12500, 16), jnp.float32)
        _rk = jax.random.fold_in(_tk, 7)
        W_top1 = 0.0693375 * jax.random.normal(jax.random.fold_in(_tk, 801), (208, 512), jnp.float32)
        W_top2 = 0.0441942 * jax.random.normal(jax.random.fold_in(_tk, 802), (512, 256), jnp.float32)
        W_top3 = 0.0625 * jax.random.normal(jax.random.fold_in(_tk, 803), (256, 1), jnp.float32)
        b_top1 = jnp.zeros((512,), jnp.float32)
        b_top2 = jnp.zeros((256,), jnp.float32)
        return (dense_ctx, ids, tbl_0, tbl_1, tbl_2, tbl_3, tbl_4, tbl_5, tbl_6, tbl_7, tbl_8, tbl_9, tbl_10, tbl_11, tbl_12, tbl_13, tbl_14, tbl_15, tbl_16, tbl_17, tbl_18, tbl_19, tbl_20, tbl_21, tbl_22, tbl_23, tbl_24, tbl_25, tbl_26, tbl_27, tbl_28, tbl_29, tbl_30, tbl_31, W_top1, b_top1, W_top2, b_top2, W_top3)
    dense_ctx, ids, tbl_0, tbl_1, tbl_2, tbl_3, tbl_4, tbl_5, tbl_6, tbl_7, tbl_8, tbl_9, tbl_10, tbl_11, tbl_12, tbl_13, tbl_14, tbl_15, tbl_16, tbl_17, tbl_18, tbl_19, tbl_20, tbl_21, tbl_22, tbl_23, tbl_24, tbl_25, tbl_26, tbl_27, tbl_28, tbl_29, tbl_30, tbl_31, W_top1, b_top1, W_top2, b_top2, W_top3 = _rec_inputs()

    def _L0_rec_setup():
        import jax, jax.numpy as jnp
        import numpy as np
        B, M, D = (2048, 32, 16)
        LAYERS = [64, 64, 64]
        key = jax.random.key(seed)
        ks = jax.random.split(key, 4)
        inp = {'embeddings': jax.random.normal(ks[0], (B, M, D), dtype=jnp.float32)}
        hk_1 = M
        for i, hk in enumerate(LAYERS):
            scale = (2.0 / (M * hk_1 + hk)) ** 0.5
            inp[f'W{i}'] = jax.random.normal(ks[i + 1], (M, hk_1, hk), dtype=jnp.float32) * scale
            hk_1 = hk
        return inp
    _L0_rec_all = _L0_rec_setup()
    _L0_rec_in = {k: v for k, v in _L0_rec_all.items() if k in ('W0', 'W1', 'W2')}
    del _L0_rec_all
    return {'dense_ctx': dense_ctx, 'ids': ids, 'tbl_0': tbl_0, 'tbl_1': tbl_1, 'tbl_2': tbl_2, 'tbl_3': tbl_3, 'tbl_4': tbl_4, 'tbl_5': tbl_5, 'tbl_6': tbl_6, 'tbl_7': tbl_7, 'tbl_8': tbl_8, 'tbl_9': tbl_9, 'tbl_10': tbl_10, 'tbl_11': tbl_11, 'tbl_12': tbl_12, 'tbl_13': tbl_13, 'tbl_14': tbl_14, 'tbl_15': tbl_15, 'tbl_16': tbl_16, 'tbl_17': tbl_17, 'tbl_18': tbl_18, 'tbl_19': tbl_19, 'tbl_20': tbl_20, 'tbl_21': tbl_21, 'tbl_22': tbl_22, 'tbl_23': tbl_23, 'tbl_24': tbl_24, 'tbl_25': tbl_25, 'tbl_26': tbl_26, 'tbl_27': tbl_27, 'tbl_28': tbl_28, 'tbl_29': tbl_29, 'tbl_30': tbl_30, 'tbl_31': tbl_31, 'W_top1': W_top1, 'b_top1': b_top1, 'W_top2': W_top2, 'b_top2': b_top2, 'W_top3': W_top3, 'L0_rec_W0': _L0_rec_in['W0'], 'L0_rec_W1': _L0_rec_in['W1'], 'L0_rec_W2': _L0_rec_in['W2']}

def reference(dense_ctx, ids, tbl_0, tbl_1, tbl_2, tbl_3, tbl_4, tbl_5, tbl_6, tbl_7, tbl_8, tbl_9, tbl_10, tbl_11, tbl_12, tbl_13, tbl_14, tbl_15, tbl_16, tbl_17, tbl_18, tbl_19, tbl_20, tbl_21, tbl_22, tbl_23, tbl_24, tbl_25, tbl_26, tbl_27, tbl_28, tbl_29, tbl_30, tbl_31, W_top1, b_top1, W_top2, b_top2, W_top3, L0_rec_W0, L0_rec_W1, L0_rec_W2):
    import jax
    import jax.numpy as jnp

    def _L0_rec_ref(embeddings, W0, W1, W2):
        import jax, jax.numpy as jnp
        import numpy as np
        B, M, D = (2048, 32, 16)
        LAYERS = [64, 64, 64]
        x0 = embeddings
        xk = x0
        outs = []
        for W in (W0, W1, W2):
            xk = jax.nn.relu(jnp.einsum('bmd,bhd,mhk->bkd', x0, xk, W))
            outs.append(jnp.sum(xk, axis=2))
        return jnp.concatenate(outs, axis=1)
    e = jnp.stack([tbl_0[ids[:, 0]], tbl_1[ids[:, 1]], tbl_2[ids[:, 2]], tbl_3[ids[:, 3]], tbl_4[ids[:, 4]], tbl_5[ids[:, 5]], tbl_6[ids[:, 6]], tbl_7[ids[:, 7]], tbl_8[ids[:, 8]], tbl_9[ids[:, 9]], tbl_10[ids[:, 10]], tbl_11[ids[:, 11]], tbl_12[ids[:, 12]], tbl_13[ids[:, 13]], tbl_14[ids[:, 14]], tbl_15[ids[:, 15]], tbl_16[ids[:, 16]], tbl_17[ids[:, 17]], tbl_18[ids[:, 18]], tbl_19[ids[:, 19]], tbl_20[ids[:, 20]], tbl_21[ids[:, 21]], tbl_22[ids[:, 22]], tbl_23[ids[:, 23]], tbl_24[ids[:, 24]], tbl_25[ids[:, 25]], tbl_26[ids[:, 26]], tbl_27[ids[:, 27]], tbl_28[ids[:, 28]], tbl_29[ids[:, 29]], tbl_30[ids[:, 30]], tbl_31[ids[:, 31]]], axis=1)
    z = _L0_rec_ref(e, L0_rec_W0, L0_rec_W1, L0_rec_W2)
    z = z.reshape(z.shape[0], -1)
    h = jnp.concatenate([z, dense_ctx], axis=1)
    h = jnp.maximum(h @ W_top1 + b_top1, 0.0)
    h = jnp.maximum(h @ W_top2 + b_top2, 0.0)
    y = h @ W_top3
    return y

_drawn_inputs = setup_inputs


def setup_inputs(seed=0):
    import zlib

    import numpy as np

    out = dict(_drawn_inputs(seed))
    spreads = {'b_top1': (0.0, 2.0), 'b_top2': (0.0, 0.8)}
    factors = {'tbl_0': 8.0,
     'tbl_1': 8.0,
     'tbl_2': 8.0,
     'tbl_3': 8.0,
     'tbl_4': 8.0,
     'tbl_5': 8.0,
     'tbl_6': 8.0,
     'tbl_7': 8.0,
     'tbl_8': 8.0,
     'tbl_9': 8.0,
     'tbl_10': 8.0,
     'tbl_11': 8.0,
     'tbl_12': 8.0,
     'tbl_13': 8.0,
     'tbl_14': 8.0,
     'tbl_15': 8.0,
     'tbl_16': 8.0,
     'tbl_17': 8.0,
     'tbl_18': 8.0,
     'tbl_19': 8.0,
     'tbl_20': 8.0,
     'tbl_21': 8.0,
     'tbl_22': 8.0,
     'tbl_23': 8.0,
     'tbl_24': 8.0,
     'tbl_25': 8.0,
     'tbl_26': 8.0,
     'tbl_27': 8.0,
     'tbl_28': 8.0,
     'tbl_29': 8.0,
     'tbl_30': 8.0,
     'tbl_31': 8.0,
     'L0_rec_W0': 3.649,
     'L0_rec_W1': 8.0,
     'L0_rec_W2': 8.0,
     'dense_ctx': 7.424}
    for name, (base, spread) in spreads.items():
        noise = np.random.default_rng([zlib.crc32(name.encode()), seed]).standard_normal(out[name].shape)
        drawn = base * np.exp(spread * noise) if base else spread * noise
        out[name] = jnp.asarray(drawn.astype(out[name].dtype))
    for name, factor in factors.items():
        out[name] = (out[name] * factor).astype(out[name].dtype)
    return out
```

```python
from contextlib import ExitStack

import concourse.bass as bass
from concourse import mybir

F32 = mybir.dt.float32
I32 = mybir.dt.int32
ALU = mybir.AluOpType
ACT = mybir.ActivationFunctionType
AXIS_X = mybir.AxisListType.X

P = 128
POOL_PAIRS = (2, 5)
EARLY_COPIES = (0, 1)
LATE_COPIES = (6, 7)
Z_SLOTS = 4
ZP_SLOTS = 2


def cin_tower(nc, dense_t, ids, tables, w0, w1, w2, wt1, bt1, wt2, bt2, wt3, out):
    DENSE, B = dense_t.shape
    M, H, K = w0.shape
    D = tables[0].shape[1]
    TILES = B // P
    HALVES = 2
    ND = D // HALVES
    N = ND * P
    NH = N // 2
    ROW = D * P
    CH = M * K // P
    PAIRS = CH // 2
    CH0 = (M // 2) * M // P
    EXTRA = P // (M // 2)
    NE = N // EXTRA
    F1 = wt1.shape[1]
    F2 = wt2.shape[1]
    JC1, JC2 = F1 // P, F2 // P
    GRP = M * D // P
    BLOCKS = TILES * HALVES
    dve_pairs = [j for j in range(PAIRS) if j not in POOL_PAIRS]
    ND_P, NP_P = len(dve_pairs), len(POOL_PAIRS)
    SHARED = 3
    GATHERED = (0, 6, 16, 23, M)
    assert M == 32

    DVE0 = CH0 // 2
    DVE_PH = 2 * ND_P + CH0 // 2
    POOL_PH = 2 * NP_P
    assert DVE_PH * 2 % Z_SLOTS == 0 and POOL_PH % ZP_SLOTS == 0

    with ExitStack() as ctx:
        def sb(name, shape, dt=F32):
            return ctx.enter_context(nc.sbuf_tensor(name, shape, dt))

        def ps(name, shape):
            return ctx.enter_context(nc.psum_tensor(name, shape, F32))

        def sem(name):
            return ctx.enter_context(nc.semaphore(name))

        x0t = nc.dram_tensor("x0t", [TILES * 2 * M, ROW], F32, kind="Internal")
        w0h = nc.dram_tensor("w0h", [M * 2 * H, K], F32, kind="Internal")
        w0m = nc.dram_tensor("w0m", [2 * M * H, K], F32, kind="Internal")

        x0b_own = [[sb(f"x0b_{s}_{j}", [P, 2, N]) for j in range(SHARED)] for s in range(HALVES)]
        x0b_shared = [sb(f"x0b_{j}", [P, 2, N]) for j in range(SHARED, PAIRS)]
        x0_rep = sb("x0_rep", [P, N])
        x0_rot = sb("x0_rot", [P, CH0, N])
        x0_lo = sb("x0_lo", [P, NE])
        x0_hi = sb("x0_hi", [P, NE])
        z_dve = sb("z_dve", [P, Z_SLOTS, 2, N])
        z_pool = sb("z_pool", [P, ZP_SLOTS, 2, N])
        z_extra = sb("z_extra", [P, NE])
        xs = [sb(f"xs{i}", [P, N]) for i in range(2)]
        relu = sb("relu", [P, 2, NH])
        zpart = sb("zpart", [P, 3, P])
        zsum = sb("zsum", [P, 3, P])
        w_sym = sb("w_sym", [P, CH0, K])
        w_symb = z_pool[:, 0, 0, 0:CH0 * K].rearrange("p (c k) -> p c k", k=K)
        w_ex = sb("w_ex", [P, K])
        w_exb = sb("w_exb", [P, K])
        w_extra = sb("w_extra", [P, EXTRA, K])
        w_cin = [sb(f"w_cin{i}", [P, CH, K]) for i in range(2)]
        wt1_z = sb("wt1_z", [P, 3, F1])
        wt1_d = sb("wt1_d", [DENSE, F1])
        wt2_s = sb("wt2_s", [P, JC1, F2])
        wt3_s = sb("wt3_s", [P, JC2])
        bt1_s = sb("bt1_s", [P, JC1])
        bt2_s = sb("bt2_s", [P, JC2])
        ids_all = sb("ids_all", [P, TILES, M], I32)
        ids_cur = sb("ids_cur", [P, M], I32)
        emb = sb("emb", [P, M * D])
        emb_t = sb("emb_t", [P, GRP, P])
        dense_s = sb("dense_s", [DENSE, P])
        ident = sb("ident", [P, P])
        h1 = sb("h1", [P, JC1, P])
        h2 = sb("h2", [P, JC2, P])
        y_row = sb("y_row", [1, P])

        acc = [ps(f"acc{i}", [P, NH]) for i in range(2)]
        xp = [ps(f"xp{i}", [P, N]) for i in range(2)]
        ps_a = ps("ps_a", [P, 512])
        ps_b = ps("ps_b", [P, 512])

        ids_in = sem("ids_in")
        dense_in = sem("dense_in")
        w0_copied = sem("w0_copied")
        w0_in = sem("w0_in")
        w1_in = sem("w1_in")
        w2_in = sem("w2_in")
        mlp_in = sem("mlp_in")
        x0b_own_in = [[sem(f"x0b_in_{s}_{j}") for j in range(SHARED)] for s in range(HALVES)]
        x0b_shared_in = [sem(f"x0b_in_{j}") for j in range(SHARED, PAIRS)]
        early_copied = sem("early_copied")
        late_copied = sem("late_copied")
        l0a_in = sem("l0a_in")
        l0b_in = sem("l0b_in")
        x0t_written = sem("x0t_written")
        out_written = sem("out_written")
        ident_zeroed = sem("ident_zeroed")
        ident_ready = sem("ident_ready")
        ids_picked = sem("ids_picked")
        gathered = sem("gathered")
        emb_transposed = sem("emb_transposed")
        emb_copied = sem("emb_copied")
        w_summed = sem("w_summed")
        w_masked = sem("w_masked")
        w_ready = sem("w_ready")
        zd_made = sem("zd_made")
        zd_used = sem("zd_used")
        zp_made = sem("zp_made")
        zp_used = sem("zp_used")
        ze_made = sem("ze_made")
        ze_used = sem("ze_used")
        xp_ready = [sem(f"xp{i}_ready") for i in range(2)]
        xs_ready = [sem(f"xs{i}_ready") for i in range(2)]
        relu_ready = sem("relu_ready")
        relu_reduced = sem("relu_reduced")
        zsum_ready = sem("zsum_ready")
        h1_done = sem("h1_done")
        h1_relu = sem("h1_relu")
        h2_done = sem("h2_done")
        h2_relu = sem("h2_relu")
        y_done = sem("y_done")
        y_copied = sem("y_copied")

        def x0b(s, j):
            return x0b_own[s][j] if j < SHARED else x0b_shared[j - SHARED]

        def x0b_ready(t, s, j):
            for copies, copied in ((EARLY_COPIES, early_copied), (LATE_COPIES, late_copied)):
                if j in copies:
                    return copied, (2 * t + s) * len(copies) + copies.index(j) + 1
            return x0b_in(t, s, j)

        def x0b_in(t, s, j):
            if j < SHARED:
                return x0b_own_in[s][j], 32 * (t + 1)
            return x0b_shared_in[j - SHARED], 32 * (2 * t + s + 1)

        def phase(t, s):
            return t * HALVES + s

        def after_l1(last):
            return ND_P + (0 if last else CH0 // 2)

        def dve_count(t, s, k):
            return phase(t, s) * DVE_PH + DVE0 + k

        def pool_count(t, s, k):
            return phase(t, s) * POOL_PH + k

        def sections(t, s, k):
            return phase(t, s) * 3 + 1 + k

        def slot_dve(s, k):
            return (s * DVE_PH + DVE0 + k) % Z_SLOTS

        block = ctx.enter_context(nc.Block())

        @block.sync
        def _(sp):
            def x0_rows(t, s, row, dims, col=0):
                off = t * (2 * M * ROW) + (row * ROW + s * N + col)
                return bass.AP(x0t, off, dims)

            def load_pair(t, s, j):
                s_in, _v = x0b_in(t, s, j)
                rows = K // 2 if j in EARLY_COPIES + LATE_COPIES else K
                for mi in range(2):
                    sp.dma_start(x0b(s, j)[K * mi:K * mi + rows, :, :],
                                 x0_rows(t, s, 4 * j + mi, [[0, rows], [2 * ROW, 2], [1, N]])).then_inc(s_in, 16)

            def load_l0(t, s):
                sp.dma_start(x0_rep[:, :], x0_rows(t, s, 0, [[0, 4], [ROW, M], [1, N]])).then_inc(l0a_in, 16)
                for c in range(CH0):
                    sp.dma_start(x0_rot[:, c, :], x0_rows(t, s, 4 * c, [[ROW, 4], [ROW, M], [1, N]])
                                 ).then_inc(l0a_in if c < 2 else l0b_in, 16)
                sp.dma_start(x0_lo[:, :],
                             x0_rows(t, s, 0, [[NE, EXTRA], [ROW, M // 2], [1, NE]])).then_inc(l0b_in, 16)
                sp.dma_start(x0_hi[:, :],
                             x0_rows(t, s, M // 2, [[NE, EXTRA], [ROW, M // 2], [1, NE]])).then_inc(l0b_in, 16)

            def wait_pair_used(t, s, k_before, j):
                layer = 0 if k_before == 0 else 1
                if j in POOL_PAIRS:
                    sp.wait_ge(zp_made, pool_count(t, s, layer * NP_P + POOL_PAIRS.index(j) + 1))
                else:
                    sp.wait_ge(zd_made, dve_count(t, s, k_before + dve_pairs.index(j) + 1))

            def load_dense(t):
                if not (isinstance(t, int) and t == 0):
                    sp.wait_ge(h1_done, t)
                sp.dma_start(dense_s[:, :], bass.AP(dense_t.tensor, t * P, [[B, DENSE], [1, P]])).then_inc(dense_in, 16)

            def loads(t, s):
                nt, ns = (t, 1) if s == 0 else (t + 1, 0)
                first = isinstance(t, int) and t == 0 and s == 0
                for j in range(SHARED):
                    if not first:
                        pt, p_s = (t, 0) if s == 1 else (t - 1, 1)
                        wait_pair_used(pt, p_s, after_l1(False), j)
                    load_pair(nt, ns, j)
                for j in range(SHARED, PAIRS):
                    wait_pair_used(t, s, after_l1(False), j)
                    load_pair(nt, ns, j)
                if not (isinstance(t, int) and phase(t, s) >= BLOCKS - 2):
                    sp.wait_ge(ze_made, phase(t, s) + 2)
                    sp.wait_ge(x0t_written, 32 * (t + 2))
                    load_l0(t + 1, s)

            sp.dma_start(ids_all[:, :, :], ids.rearrange("(t p) f -> p t f", p=P)).then_inc(ids_in, 16)
            sp.wait_ge(x0t_written, 32)
            load_l0(0, 0)
            for j in range(PAIRS):
                load_pair(0, 0, j)
            sp.wait_ge(zd_made, DVE0)
            sp.wait_ge(ze_made, 1)
            load_l0(0, 1)
            loads(0, 0)
            loads(0, 1)
            load_dense(0)
            with sp.Fori(1, TILES - 1) as t:
                loads(t, 0)
                loads(t, 1)
                load_dense(t)
            loads(TILES - 1, 0)
            load_dense(TILES - 1)
            sp.wait_ge(out_written, 16 * TILES)

        @block.gpsimd
        def _(pool):
            def pick_ids(t):
                nc.gpsimd.tensor_copy(ids_cur[:, :], ids_all[:, t, :]).then_inc(ids_picked, 1)
                pool.wait_ge(ids_picked, t + 1)

            def gather(f0, f1):
                for f in range(f0, f1):
                    nc.gpsimd.indirect_dma_start(
                        out=emb[:, D * f:D * f + D], out_offset=None, in_=tables[f],
                        in_offset=bass.IndirectOffsetOnAxis(ap=ids_cur[:, f:f + 1], axis=0)).then_inc(gathered, 16)

            def multiply(t, s, layer, i):
                j = POOL_PAIRS[i]
                k = layer * NP_P + i
                s_in, v = x0b_ready(t, s, j)
                pool.wait_ge(s_in, v)
                if i == 0:
                    pool.wait_ge(xs_ready[layer], phase(t, s) + 1)
                if not (isinstance(t, int) and phase(t, s) == 0 and k < ZP_SLOTS):
                    pool.wait_ge(zp_used, pool_count(t, s, k + 1 - ZP_SLOTS))
                nc.gpsimd.tensor_tensor(z_pool[:, k % ZP_SLOTS, :, :], x0b(s, j)[:, :, :],
                                        xs[layer][:, :].unsqueeze(1).broadcast_to([P, 2, N]),
                                        ALU.mult).then_inc(zp_made, 1)

            def body(t, last_tile, next_last):
                for s in range(HALVES):
                    for layer in range(2):
                        stage = 2 * s + layer
                        multiply(t, s, layer, 0)
                        if stage == 1 and not next_last:
                            pool.wait_ge(emb_transposed, t + 2)
                            pick_ids(t + 2)
                        multiply(t, s, layer, 1)
                        if stage == 0 and not last_tile:
                            gather(GATHERED[3], GATHERED[4])
                        elif stage > 0 and not next_last:
                            gather(GATHERED[stage - 1], GATHERED[stage])

            nc.gpsimd.memset(ident[:, :], 0.0).then_inc(ident_zeroed, 1)
            pool.wait_ge(ident_zeroed, 1)
            nc.gpsimd.affine_select(out=ident[:, :], in_=ident[:, :], compare_op=ALU.not_equal, fill=1.0, base=0,
                                    pattern=[[-1, P]], channel_multiplier=1).then_inc(ident_ready, 1)
            pool.wait_ge(ids_in, 16)
            pick_ids(0)
            gather(0, M)
            pool.wait_ge(w_summed, 2)
            half = M // 2
            nc.gpsimd.affine_select(out=w_extra[:, :, :], in_=w_ex[:, :].unsqueeze(1).broadcast_to([P, EXTRA, K]),
                                    compare_op=ALU.is_ge, fill=0.0, base=0,
                                    pattern=[[-half, EXTRA], [0, K]], channel_multiplier=1).then_inc(w_masked, 1)
            pool.wait_ge(w_masked, 1)
            nc.gpsimd.affine_select(out=w_extra[:, :, :], in_=w_extra[:, :, :],
                                    compare_op=ALU.is_ge, fill=0.0, base=half - 1,
                                    pattern=[[half, EXTRA], [0, K]], channel_multiplier=-1).then_inc(w_ready, 1)
            pool.wait_ge(emb_transposed, 1)
            pick_ids(1)
            gather(0, GATHERED[3])
            body(0, False, False)
            with pool.Fori(1, TILES - 2) as t:
                body(t, False, False)
            body(TILES - 2, False, True)
            body(TILES - 1, True, True)

        @block.vector
        def _(dve):
            def product(t, s, k, in0, in1):
                if not (isinstance(t, int) and DVE_PH * phase(t, s) + DVE0 + k < Z_SLOTS):
                    dve.wait_ge(zd_used, dve_count(t, s, k + 1 - Z_SLOTS))
                nc.vector.tensor_tensor(z_dve[:, slot_dve(s, k), :, :], in0, in1, ALU.mult).then_inc(zd_made, 1)

            def cin_pair(t, s, layer, i, k):
                j = dve_pairs[i]
                s_in, v = x0b_ready(t, s, j)
                dve.wait_ge(s_in, v)
                if i == 0:
                    dve.wait_ge(xp_ready[layer], phase(t, s) + 1)
                product(t, s, k, xp[layer][:, :].unsqueeze(1).broadcast_to([P, 2, N]), x0b(s, j)[:, :, :])

            def layer0(t, s, k, block_no):
                dve.wait_ge(l0a_in, 3 * 16 * (block_no + 1))
                for i in range(CH0 // 2):
                    if i == 1:
                        dve.wait_ge(l0b_in, (CH0 - 2 + 2) * 16 * (block_no + 1))
                    product(t, s, k + i, x0_rep[:, :].unsqueeze(1).broadcast_to([P, 2, N]),
                            x0_rot[:, 2 * i:2 * i + 2, :])
                if not (isinstance(block_no, int) and block_no == 0):
                    dve.wait_ge(ze_used, block_no)
                nc.vector.tensor_tensor(z_extra[:, :], x0_lo[:, :], x0_hi[:, :], ALU.mult).then_inc(ze_made, 1)

            def reduce(t, s, l, n, slot):
                part = (zpart, zsum)[s]
                dve.wait_ge(relu_ready, n)
                if s == 1 and l == 0 and not (isinstance(t, int) and t == 0):
                    dve.wait_ge(h1_done, t)
                nc.vector.tensor_reduce(part[:, l, :],
                                        relu[:, slot, :].rearrange("p (d b) -> p b d", b=P),
                                        AXIS_X, ALU.add).then_inc(relu_reduced, 1)
                if s == 1:
                    dve.wait_ge(relu_reduced, n)
                    nc.vector.tensor_tensor(zsum[:, l, :], zpart[:, l, :], zsum[:, l, :],
                                            ALU.add).then_inc(zsum_ready, 1)

            def body(t, first_tile, last_tile):
                for s in range(HALVES):
                    last = last_tile and s == 1
                    k = 0
                    for i in range(ND_P):
                        cin_pair(t, s, 0, i, k)
                        k += 1
                        if i == 3 and first_tile and s == 0:
                            reduce(0, 0, 0, 1, 0)
                        elif i == 3:
                            pt, p_s = (t, 0) if s == 1 else (t - 1, 1)
                            reduce(pt, p_s, 2, sections(t, s, 0), (3 * s + 0) % 2)
                    if not last:
                        layer0(t, s, k, phase(t, s) + 1)
                        k += CH0 // 2
                    for i in range(ND_P):
                        cin_pair(t, s, 1, i, k)
                        k += 1
                        if i == 1:
                            reduce(t, s, 1, sections(t, s, 1), (3 * s + 1) % 2)
                        if i == 3 and not last:
                            nt, ns = (t, 1) if s == 0 else (t + 1, 0)
                            reduce(nt, ns, 0, sections(t, s, 2), (3 * s + 2) % 2)

            dve.wait_ge(w0_in, 10 * 16)
            nc.vector.tensor_tensor(w_ex[:, :], w_ex[:, :], w_exb[:, :], ALU.add).then_inc(w_summed, 1)
            nc.vector.tensor_tensor(w_sym[:, :, :], w_sym[:, :, :], w_symb[:, :, :], ALU.add).then_inc(w_summed, 1)
            dve.wait_ge(w_summed, 2)
            nc.vector.tensor_scalar(w_sym[0:M, 0, :], w_sym[0:M, 0, :], 0.5, None, ALU.mult).then_inc(w_ready, 1)
            layer0(0, 0, -DVE0, 0)
            body(0, True, False)
            with dve.Fori(1, TILES - 1) as t:
                body(t, False, False)
            body(TILES - 1, False, True)
            last_sections = sections(TILES - 1, 1, 0) + 2
            reduce(TILES - 1, 1, 2, last_sections, (last_sections - 1) % 2)

        @block.scalar
        def _(act):
            def wait_l0(block_no):
                act.wait_ge(ze_used, block_no + 1)

            def wait_layer(t, s, k):
                act.wait_ge(zd_used, dve_count(t, s, k))

            def spread(t, s, layer, n, slot):
                for buf, ready in ((xp[layer], xp_ready[layer]), (xs[layer], xs_ready[layer])):
                    if not (isinstance(t, int) and phase(t, s) == 0):
                        pt, p_s = (t, 0) if s == 1 else (t - 1, 1)
                        if buf is xp[layer]:
                            k = ND_P if layer == 0 else DVE_PH
                            act.wait_ge(zd_made, dve_count(pt, p_s, k))
                        else:
                            act.wait_ge(zp_made, pool_count(pt, p_s, NP_P * (layer + 1)))
                    for copy in range(2):
                        for side in range(2):
                            ins = nc.scalar.activation(buf[K * copy:K * copy + K, NH * side:NH * side + NH],
                                                       acc[slot][K * side:K * side + K, :], ACT.Relu)
                    ins.then_inc(ready, 1)
                sum_input(n, slot)

            def sum_input(n, slot):
                if not (isinstance(n, int) and n <= 2):
                    act.wait_ge(relu_reduced, n - 2)
                nc.scalar.activation(relu[:, slot, :], acc[slot][:, :], ACT.Relu).then_inc(relu_ready, 1)

            def copy_x0(t, s, copies, copied, which):
                for j in copies:
                    if j not in which:
                        continue
                    s_in, v = x0b_in(t, s, j)
                    act.wait_ge(s_in, v)
                    for mi in range(2):
                        ins = nc.scalar.copy(x0b(s, j)[K * mi + K // 2:K * mi + K, :, :],
                                             x0b(s, j)[K * mi:K * mi + K // 2, :, :])
                    ins.then_inc(copied, 1)

            def write_x0t(t):
                act.wait_ge(emb_transposed, t + 1)
                if not (isinstance(t, int) and t == 0):
                    act.wait_ge(x0t_written, 32 * t)
                nc.scalar.copy(emb_t[:, :, :], ps_b[:, :].rearrange("p (g b) -> p g b", g=GRP)).then_inc(emb_copied, 1)
                act.wait_ge(emb_copied, t + 1)
                for rep in range(2):
                    act.dma_start(bass.AP(x0t, t * (2 * M * ROW) + rep * M * ROW, [[P, P], [P * P, GRP], [1, P]]),
                                  emb_t[:, :, :]).then_inc(x0t_written, 16)

            def h1_out(t):
                act.wait_ge(h1_done, t + 1)
                for jc in range(JC1):
                    ins = nc.scalar.activation(h1[:, jc, :], ps_a[:, P * jc:P * jc + P], ACT.Relu,
                                               bias=bt1_s[:, jc:jc + 1])
                ins.then_inc(h1_relu, 1)

            def h2_out(t):
                act.wait_ge(h2_done, t + 1)
                for jc in range(JC2):
                    ins = nc.scalar.activation(h2[:, jc, :], ps_b[:, P * jc:P * jc + P], ACT.Relu,
                                               bias=bt2_s[:, jc:jc + 1])
                ins.then_inc(h2_relu, 1)

            def y_out(t):
                act.wait_ge(y_done, t + 1)
                nc.scalar.copy(y_row[0:1, :], ps_a[0:1, 0:P]).then_inc(y_copied, 1)
                act.wait_ge(y_copied, t + 1)
                act.dma_start(bass.AP(out.tensor, t * P, [[P, 1], [1, P]]), y_row[0:1, :]).then_inc(out_written, 16)

            def body(t, first_tile, last_tile):
                for s in range(HALVES):
                    last = last_tile and s == 1
                    base = 3 * s
                    copy_x0(t, s, LATE_COPIES, late_copied, LATE_COPIES)
                    wait_layer(t, s, ND_P)
                    spread(t, s, 1, sections(t, s, 1), (base + 1) % 2)
                    if s == 0 and not first_tile:
                        h1_out(t - 1)
                    if s == 1 and not first_tile:
                        y_out(t - 1)
                    if not last:
                        nt, ns = (t, 1) if s == 0 else (t + 1, 0)
                        wait_l0(phase(t, s) + 1)
                        spread(nt, ns, 0, sections(t, s, 2), (base + 2) % 2)
                    if s == 0 and not last_tile:
                        write_x0t(t + 1)
                    if not last:
                        copy_x0(nt, ns, EARLY_COPIES, early_copied, EARLY_COPIES)
                    n = sections(t, s, 3) if not last else sections(t, s, 2)
                    slot = (base + 3) % 2 if not last else (base + 2) % 2
                    wait_layer(t, s, after_l1(last) + ND_P)
                    sum_input(n, slot)
                    if s == 0 and not first_tile:
                        h2_out(t - 1)
                if not first_tile:
                    act.wait_ge(out_written, 16 * t)

            for rep in range(2):
                act.dma_start(bass.AP(w0h, rep * H * K, [[2 * H * K, M], [1, H * K]]),
                              w0.rearrange("m h k -> m (h k)")).then_inc(w0_copied, 16)
                act.dma_start(bass.AP(w0m, rep * M * H * K, [[H * K, M], [1, H * K]]),
                              w0.rearrange("m h k -> m (h k)")).then_inc(w0_copied, 16)
            act.wait_ge(w0_copied, 64)
            act.dma_start(w_ex[:, :], bass.AP(w0h, (M // 2) * K,
                                              [[0, EXTRA], [(2 * H + 1) * K, M // 2], [1, K]])).then_inc(w0_in, 16)
            act.dma_start(w_exb[:, :], bass.AP(w0m, (M // 2) * H * K,
                                               [[0, EXTRA], [(H + 1) * K, M // 2], [1, K]])).then_inc(w0_in, 16)
            for q in range(4):
                act.dma_start(w_sym[M * q:M * q + M, :, :],
                              bass.AP(w0h, q * K, [[(2 * H + 1) * K, M], [4 * K, CH0], [1, K]])).then_inc(w0_in, 16)
                act.dma_start(w_symb[M * q:M * q + M, :, :],
                              bass.AP(w0m, q * H * K, [[(H + 1) * K, M], [4 * H * K, CH0], [1, K]])
                              ).then_inc(w0_in, 16)
            act.dma_start(w_cin[0][:, :, :],
                          w1.rearrange("m h k -> (m h) k").rearrange("(c p) k -> p c k", p=P)).then_inc(w1_in, 16)
            act.dma_start(w_cin[1][:, :, :],
                          w2.rearrange("m h k -> (m h) k").rearrange("(c p) k -> p c k", p=P)).then_inc(w2_in, 16)
            for copy in range(2):
                act.dma_start(wt1_z[K * copy:K * copy + K, :, :],
                              wt1[0:3 * K, :].rearrange("(l k) j -> k l j", k=K)).then_inc(mlp_in, 16)
            act.dma_start(wt1_d[:, :], wt1[3 * K:3 * K + DENSE, :]).then_inc(mlp_in, 16)
            act.dma_start(wt2_s[:, :, :], wt2.rearrange("(p c) j -> p c j", p=P)).then_inc(mlp_in, 16)
            act.dma_start(wt3_s[:, :], wt3.rearrange("(p c) o -> p (c o)", p=P)).then_inc(mlp_in, 16)
            act.dma_start(bt1_s[:, :], bt1.rearrange("(p c) -> p c", p=P)).then_inc(mlp_in, 16)
            act.dma_start(bt2_s[:, :], bt2.rearrange("(p c) -> p c", p=P)).then_inc(mlp_in, 16)
            write_x0t(0)
            act.wait_ge(mlp_in, 7 * 16)
            copy_x0(0, 0, EARLY_COPIES, early_copied, EARLY_COPIES[:1])
            wait_l0(0)
            spread(0, 0, 0, 1, 0)
            copy_x0(0, 0, EARLY_COPIES, early_copied, EARLY_COPIES[1:])
            body(0, True, False)
            with act.Fori(1, TILES - 1) as t:
                body(t, False, False)
            body(TILES - 1, False, True)
            h1_out(TILES - 1)
            h2_out(TILES - 1)
            y_out(TILES - 1)

        @block.tensor
        def _(pe):
            def claim(n, slot):
                if not (isinstance(n, int) and n <= 2):
                    pe.wait_ge(relu_ready, n - 2)

            def pair(a, z, weights, chunk0, start, stop):
                for c in range(2):
                    for side in range(2):
                        ins = nc.tensor.matmul(a[K * side:K * side + K, :], weights[:, chunk0 + c, :],
                                               z[:, c, NH * side:NH * side + NH],
                                               start=start and c == 0, stop=stop and c == 1)
                return ins

            def layer0(t, s, k, n, slot, block_no):
                a = acc[slot]
                claim(n, slot)
                for i in range(CH0 // 2):
                    pe.wait_ge(zd_made, dve_count(t, s, k + i + 1))
                    pair(a, z_dve[:, slot_dve(s, k + i), :, :], w_sym, 2 * i, i == 0, False).then_inc(zd_used, 1)
                pe.wait_ge(ze_made, block_no + 1)
                for e in range(EXTRA // 2):
                    for side in range(2):
                        ins = nc.tensor.matmul(a[K * side:K * side + K, NE * e:NE * e + NE],
                                               w_extra[:, EXTRA // 2 * side + e, :], z_extra[:, :],
                                               start=False, stop=e == EXTRA // 2 - 1)
                ins.then_inc(ze_used, 1)

            def layer(t, s, l, k, n, slot):
                claim(n, slot)
                kd, kp = k, l * NP_P
                for j in range(PAIRS):
                    if j in POOL_PAIRS:
                        pe.wait_ge(zp_made, pool_count(t, s, kp + 1))
                        z, used = z_pool[:, kp % ZP_SLOTS, :, :], zp_used
                        kp += 1
                    else:
                        pe.wait_ge(zd_made, dve_count(t, s, kd + 1))
                        z, used = z_dve[:, slot_dve(s, kd), :, :], zd_used
                        kd += 1
                    ins = pair(acc[slot], z, w_cin[l], 2 * j, j == 0, j == PAIRS - 1)
                    ins.then_inc(used, 1)

            def transpose_tile(t):
                pe.wait_ge(gathered, 16 * M * (t + 1))
                for g in range(GRP):
                    ins = nc.tensor.transpose(ps_b[:, P * g:P * g + P], emb[:, P * g:P * g + P], ident[:, :])
                ins.then_inc(emb_transposed, 1)

            def mlp1(t):
                pe.wait_ge(zsum_ready, 3 * (t + 1))
                pe.wait_ge(dense_in, 16 * (t + 1))
                for jc in range(JC1):
                    for l in range(3):
                        nc.tensor.matmul(ps_a[:, P * jc:P * jc + P], wt1_z[:, l, jc:F1:JC1],
                                         zsum[:, l, :], start=l == 0, stop=False)
                    ins = nc.tensor.matmul(ps_a[:, P * jc:P * jc + P], wt1_d[:, jc:F1:JC1],
                                           dense_s[:, :], start=False, stop=True)
                ins.then_inc(h1_done, 1)

            def mlp2(t, emb_read):
                pe.wait_ge(h1_relu, t + 1)
                pe.wait_ge(emb_copied, emb_read)
                for jc in range(JC2):
                    for c in range(JC1):
                        ins = nc.tensor.matmul(ps_b[:, P * jc:P * jc + P], wt2_s[:, c, jc:F2:JC2],
                                               h1[:, c, :], start=c == 0, stop=c == JC1 - 1)
                ins.then_inc(h2_done, 1)

            def mlp3(t):
                pe.wait_ge(h2_relu, t + 1)
                for c in range(JC2):
                    ins = nc.tensor.matmul(ps_a[0:1, 0:P], wt3_s[:, c:c + 1], h2[:, c, :],
                                           start=c == 0, stop=c == JC2 - 1)
                ins.then_inc(y_done, 1)

            def body(t, first_tile, last_tile):
                for s in range(HALVES):
                    last = last_tile and s == 1
                    base = 3 * s
                    layer(t, s, 0, 0, sections(t, s, 1), (base + 1) % 2)
                    if not first_tile:
                        if s == 0:
                            mlp1(t - 1)
                        else:
                            mlp3(t - 1)
                    k = ND_P
                    if not last:
                        layer0(t, s, k, sections(t, s, 2), (base + 2) % 2, phase(t, s) + 1)
                        k += CH0 // 2
                    if s == 0 and not last_tile:
                        transpose_tile(t + 1)
                    n = sections(t, s, 3) if not last else sections(t, s, 2)
                    layer(t, s, 1, k, n, (base + 3) % 2 if not last else (base + 2) % 2)
                    if s == 0 and not first_tile:
                        mlp2(t - 1, t + 1 if last_tile else t + 2)
                if not first_tile:
                    pe.wait_ge(y_copied, t)

            pe.wait_ge(ident_ready, 1)
            transpose_tile(0)
            pe.wait_ge(w_ready, 2)
            layer0(0, 0, -DVE0, 1, 0, 0)
            pe.wait_ge(w1_in, 16)
            pe.wait_ge(w2_in, 16)
            pe.wait_ge(mlp_in, 7 * 16)
            body(0, True, False)
            with pe.Fori(1, TILES - 1) as t:
                body(t, False, False)
            body(TILES - 1, False, True)
            mlp1(TILES - 1)
            mlp2(TILES - 1, TILES)
            mlp3(TILES - 1)


N_TABLES = 32


def kernel(**inputs):
    import numpy as _np
    import concourse.bacc as _bacc
    from concourse import mybir as _mybir
    from concourse.bass_utils import run_bass_kernel_spmd as _run

    nc = _bacc.Bacc("TRN2", target_bir_lowering=False, num_devices=1)
    arrays = {}

    def dram(name, transposed=False):
        a = _np.ascontiguousarray(_np.asarray(inputs[name]).T if transposed else inputs[name])
        arrays[f"in_{name}_dram"] = a
        return nc.dram_tensor(f"in_{name}_dram", a.shape, _mybir.dt.from_np(a.dtype), kind="ExternalInput").ap()

    tables = [dram(f"tbl_{f}") for f in range(N_TABLES)]
    out = nc.dram_tensor("out_0_dram", (inputs["ids"].shape[0], 1), F32, kind="ExternalOutput").ap()
    cin_tower(nc, dram("dense_ctx", transposed=True), dram("ids"), tables, dram("L0_rec_W0"), dram("L0_rec_W1"), dram("L0_rec_W2"),
              dram("W_top1"), dram("b_top1"), dram("W_top2"), dram("b_top2"), dram("W_top3"), out)
    r = _run(nc, [arrays], core_ids=[0])
    return r.results[0]["out_0_dram"]
```

```python
from contextlib import ExitStack

import concourse.bass as bass
from concourse import mybir

F32 = mybir.dt.float32
I32 = mybir.dt.int32
ALU = mybir.AluOpType
ACT = mybir.ActivationFunctionType
AXIS_X = mybir.AxisListType.X

P = 128
POOL_PAIRS = (2, 5)
EARLY_COPIES = (0, 1, 3)
LATE_COPIES = (6, 7)
Z_SLOTS = 4
ZP_SLOTS = 2
WARM_L0, WARM_FIRST_X, WARM_LAST_X, WARM_LAST_Z = 7, 5, 3, 2


def cin_tower(nc, dense_t, ids, tables, w0, w1, w2, wt1, bt1, wt2, bt2, wt3, out):
    DENSE, B = dense_t.shape
    M, H, K = w0.shape
    D = tables[0].shape[1]
    TILES = B // P
    HALVES = 2
    ND = D // HALVES
    N = ND * P
    NH = N // 2
    ROW = D * P
    CH = M * K // P
    PAIRS = CH // 2
    CH0 = (M // 2) * M // P
    EXTRA = P // (M // 2)
    NE = N // EXTRA
    F1 = wt1.shape[1]
    F2 = wt2.shape[1]
    JC1, JC2 = F1 // P, F2 // P
    GRP = M * D // P
    BLOCKS = TILES * HALVES
    dve_pairs = [j for j in range(PAIRS) if j not in POOL_PAIRS]
    ND_P, NP_P = len(dve_pairs), len(POOL_PAIRS)
    SHARED = 3
    GATHERED = (13, 18, 30, M)
    assert M == 32

    DVE0 = CH0 // 2
    DVE_PH = 2 * ND_P + CH0 // 2
    POOL_PH = 2 * NP_P
    assert DVE_PH * 2 % Z_SLOTS == 0 and POOL_PH % ZP_SLOTS == 0

    with ExitStack() as ctx:
        def sb(name, shape, dt=F32):
            return ctx.enter_context(nc.sbuf_tensor(name, shape, dt))

        def ps(name, shape):
            return ctx.enter_context(nc.psum_tensor(name, shape, F32))

        def sem(name):
            return ctx.enter_context(nc.semaphore(name))

        x0t = nc.dram_tensor("x0t", [TILES * 2 * M, ROW], F32, kind="Internal")
        w0h = nc.dram_tensor("w0h", [M * 2 * H, K], F32, kind="Internal")
        w0m = nc.dram_tensor("w0m", [2 * M * H, K], F32, kind="Internal")

        x0b_own = [[sb(f"x0b_{s}_{j}", [P, 2, N]) for j in range(SHARED)] for s in range(HALVES)]
        x0b_shared = [sb(f"x0b_{j}", [P, 2, N]) for j in range(SHARED, PAIRS)]
        x0_rep = sb("x0_rep", [P, N])
        x0_rot = sb("x0_rot", [P, CH0, N])
        x0_lo = sb("x0_lo", [P, NE])
        x0_hi = sb("x0_hi", [P, NE])
        z_dve = sb("z_dve", [P, Z_SLOTS, 2, N])
        z_pool = sb("z_pool", [P, ZP_SLOTS, 2, N])
        z_extra = sb("z_extra", [P, NE])
        xs = [sb(f"xs{i}", [P, N]) for i in range(2)]
        relu = [sb("relu01", [2 * K, N]), sb("relu2", [K, N])]
        zpart = [sb("zpart01", [2 * K, P]), sb("zpart2", [K, P])]
        zsum = [sb("zsum01", [2 * K, P]), sb("zsum2_dense", [K + DENSE, P])]
        w_sym = sb("w_sym", [P, CH0, K])
        w_symb = z_pool[:, 0, 0, 0:CH0 * K].rearrange("p (c k) -> p c k", k=K)
        w_ex = sb("w_ex", [P, K])
        w_exb = sb("w_exb", [P, K])
        w_extra = sb("w_extra", [P, EXTRA, K])
        w_cin = [sb(f"w_cin{i}", [P, CH, K]) for i in range(2)]
        wt1_s = [sb("wt1_a", [2 * K, F1]), sb("wt1_b", [K + DENSE, F1])]
        wt2_s = sb("wt2_s", [P, JC1, F2])
        wt3_s = sb("wt3_s", [P, JC2])
        bt1_s = sb("bt1_s", [P, JC1])
        bt2_s = sb("bt2_s", [P, JC2])
        ids_all = sb("ids_all", [P, TILES, M], I32)
        ids_cur = sb("ids_cur", [P, M], I32)
        emb = sb("emb", [P, M * D])
        emb_t = sb("emb_t", [P, GRP, P])
        ident = sb("ident", [P, P])
        h1 = sb("h1", [P, JC1, P])
        h2 = sb("h2", [P, JC2, P])
        y_row = sb("y_row", [1, P])

        acc = [ps(f"acc{i}", [P, NH]) for i in range(2)]
        xp = [ps(f"xp{i}", [P, N]) for i in range(2)]
        ps_a = ps("ps_a", [P, 512])
        ps_b = ps("ps_b", [P, 512])

        ids_in = sem("ids_in")
        dense_in = sem("dense_in")
        w0_copied = sem("w0_copied")
        w0_in = sem("w0_in")
        w1_in = sem("w1_in")
        w2_in = sem("w2_in")
        mlp_in = sem("mlp_in")
        x0b_own_in = [[sem(f"x0b_in_{s}_{j}") for j in range(SHARED)] for s in range(HALVES)]
        x0b_shared_in = [sem(f"x0b_in_{j}") for j in range(SHARED, PAIRS)]
        early_copied = sem("early_copied")
        late_copied = sem("late_copied")
        l0a_in = sem("l0a_in")
        l0b_in = sem("l0b_in")
        x0t0_written = [sem(f"x0t0_written_{g}") for g in range(GRP)]
        x0t_written = sem("x0t_written")
        out_written = sem("out_written")
        ident_zeroed = sem("ident_zeroed")
        ident_ready = sem("ident_ready")
        ids_picked = sem("ids_picked")
        gathered0 = [sem(f"gathered0_{g}") for g in range(GRP)]
        gathered = sem("gathered")
        emb_transposed = sem("emb_transposed")
        emb0_copied = sem("emb0_copied")
        emb_copied = sem("emb_copied")
        w_summed = sem("w_summed")
        w_masked = sem("w_masked")
        w_ready = sem("w_ready")
        zd_made = sem("zd_made")
        zd_used = sem("zd_used")
        zp_made = sem("zp_made")
        zp_used = sem("zp_used")
        ze_made = sem("ze_made")
        ze_used = sem("ze_used")
        xp_ready = [sem(f"xp{i}_ready") for i in range(2)]
        xs_ready = [sem(f"xs{i}_ready") for i in range(2)]
        relu_ready = sem("relu_ready")
        relu_reduced = [sem("relu01_reduced"), sem("relu2_reduced")]
        zsum_ready = sem("zsum_ready")
        h1_done = sem("h1_done")
        h1_relu = sem("h1_relu")
        h2_done = sem("h2_done")
        h2_relu = sem("h2_relu")
        y_done = sem("y_done")
        y_copied = sem("y_copied")

        def x0b(s, j):
            return x0b_own[s][j] if j < SHARED else x0b_shared[j - SHARED]

        def x0b_ready(t, s, j):
            for copies, copied in ((EARLY_COPIES, early_copied), (LATE_COPIES, late_copied)):
                if j in copies:
                    return copied, (2 * t + s) * len(copies) + copies.index(j) + 1
            return x0b_in(t, s, j)

        def x0b_in(t, s, j):
            if j < SHARED:
                return x0b_own_in[s][j], 32 * (t + 1)
            return x0b_shared_in[j - SHARED], 32 * (2 * t + s + 1)

        def phase(t, s):
            return t * HALVES + s

        def after_l1(last):
            return ND_P + (0 if last else CH0 // 2)

        def dve_count(t, s, k):
            return phase(t, s) * DVE_PH + DVE0 + k

        def pool_count(t, s, k):
            return phase(t, s) * POOL_PH + k

        def sections(t, s, k):
            return phase(t, s) * 3 + 1 + k

        def slot_dve(s, k):
            return (s * DVE_PH + DVE0 + k) % Z_SLOTS

        block = ctx.enter_context(nc.Block())

        @block.sync
        def _(sp):
            def x0_rows(t, s, row, dims, col=0):
                off = t * (2 * M * ROW) + (row * ROW + s * N + col)
                return bass.AP(x0t, off, dims)

            def load_pair(t, s, j):
                s_in, _v = x0b_in(t, s, j)
                rows = K // 2 if j in EARLY_COPIES + LATE_COPIES else K
                for mi in range(2):
                    sp.dma_start(x0b(s, j)[K * mi:K * mi + rows, :, :],
                                 x0_rows(t, s, 4 * j + mi, [[0, rows], [2 * ROW, 2], [1, N]])).then_inc(s_in, 16)

            def load_l0(t, s):
                sp.dma_start(x0_rep[:, :], x0_rows(t, s, 0, [[0, 4], [ROW, M], [1, N]])).then_inc(l0a_in, 16)
                for c in range(CH0):
                    sp.dma_start(x0_rot[:, c, :], x0_rows(t, s, 4 * c, [[ROW, 4], [ROW, M], [1, N]])
                                 ).then_inc(l0a_in if c < 2 else l0b_in, 16)
                sp.dma_start(x0_lo[:, :],
                             x0_rows(t, s, 0, [[NE, EXTRA], [ROW, M // 2], [1, NE]])).then_inc(l0b_in, 16)
                sp.dma_start(x0_hi[:, :],
                             x0_rows(t, s, M // 2, [[NE, EXTRA], [ROW, M // 2], [1, NE]])).then_inc(l0b_in, 16)

            def wait_pair_used(t, s, k_before, j):
                layer = 0 if k_before == 0 else 1
                if j in POOL_PAIRS:
                    sp.wait_ge(zp_made, pool_count(t, s, layer * NP_P + POOL_PAIRS.index(j) + 1))
                else:
                    sp.wait_ge(zd_made, dve_count(t, s, k_before + dve_pairs.index(j) + 1))

            def load_dense(t):
                if not (isinstance(t, int) and t == 0):
                    sp.wait_ge(h1_done, t)
                sp.dma_start(zsum[1][K:K + DENSE, :], bass.AP(dense_t.tensor, t * P, [[B, DENSE], [1, P]])).then_inc(dense_in, 16)

            def loads(t, s):
                nt, ns = (t, 1) if s == 0 else (t + 1, 0)
                first = isinstance(t, int) and t == 0 and s == 0
                for j in range(SHARED):
                    if not first:
                        pt, p_s = (t, 0) if s == 1 else (t - 1, 1)
                        wait_pair_used(pt, p_s, after_l1(False), j)
                    load_pair(nt, ns, j)
                for j in range(SHARED, PAIRS):
                    wait_pair_used(t, s, after_l1(False), j)
                    load_pair(nt, ns, j)
                if not (isinstance(t, int) and phase(t, s) >= BLOCKS - 2):
                    sp.wait_ge(ze_made, phase(t, s) + 2)
                    sp.wait_ge(x0t_written, 32 * (t + 1))
                    load_l0(t + 1, s)

            sp.dma_start(ids_all[:, :, :], ids.rearrange("(t p) f -> p t f", p=P)).then_inc(ids_in, 16)
            for g in range(GRP):
                sp.wait_ge(x0t0_written[g], 32)
                if g < GRP // 2:
                    for j in range(PAIRS // GRP * g, PAIRS // GRP * (g + 1)):
                        load_pair(0, 0, j)
            load_l0(0, 0)
            for j in range(PAIRS // 2, PAIRS):
                load_pair(0, 0, j)
            sp.wait_ge(zd_made, DVE0)
            sp.wait_ge(ze_made, 1)
            load_l0(0, 1)
            loads(0, 0)
            loads(0, 1)
            load_dense(0)
            with sp.Fori(1, TILES - 1) as t:
                loads(t, 0)
                loads(t, 1)
                load_dense(t)
            loads(TILES - 1, 0)
            load_dense(TILES - 1)
            sp.wait_ge(out_written, 16 * TILES)

        @block.gpsimd
        def _(pool):
            def pick_ids(t):
                nc.gpsimd.tensor_copy(ids_cur[:, :], ids_all[:, t, :]).then_inc(ids_picked, 1)
                pool.wait_ge(ids_picked, t + 1)

            def gather(f0, f1, done=gathered):
                for f in range(f0, f1):
                    nc.gpsimd.indirect_dma_start(
                        out=emb[:, D * f:D * f + D], out_offset=None, in_=tables[f],
                        in_offset=bass.IndirectOffsetOnAxis(ap=ids_cur[:, f:f + 1], axis=0)).then_inc(done, 16)

            def multiply(t, s, layer, i):
                j = POOL_PAIRS[i]
                k = layer * NP_P + i
                s_in, v = x0b_ready(t, s, j)
                pool.wait_ge(s_in, v)
                if i == 0:
                    pool.wait_ge(xs_ready[layer], phase(t, s) + 1)
                if not (isinstance(t, int) and phase(t, s) == 0 and k < ZP_SLOTS):
                    pool.wait_ge(zp_used, pool_count(t, s, k + 1 - ZP_SLOTS))
                nc.gpsimd.tensor_tensor(z_pool[:, k % ZP_SLOTS, :, :], x0b(s, j)[:, :, :],
                                        xs[layer][:, :].unsqueeze(1).broadcast_to([P, 2, N]),
                                        ALU.mult).then_inc(zp_made, 1)

            def body(t, last_tile, next_last):
                for s in range(HALVES):
                    for layer in range(2):
                        stage = 2 * s + layer
                        multiply(t, s, layer, 0)
                        if stage == 2 and not next_last:
                            pool.wait_ge(emb_transposed, GRP * (t + 2))
                            pick_ids(t + 2)
                        multiply(t, s, layer, 1)
                        if s == 0 and not last_tile:
                            gather(GATHERED[layer + 1], GATHERED[layer + 2])
                        elif s == 1 and not next_last:
                            gather(GATHERED[0] if layer else 0, GATHERED[layer])

            nc.gpsimd.memset(ident[:, :], 0.0).then_inc(ident_zeroed, 1)
            pool.wait_ge(ident_zeroed, 1)
            nc.gpsimd.affine_select(out=ident[:, :], in_=ident[:, :], compare_op=ALU.not_equal, fill=1.0, base=0,
                                    pattern=[[-1, P]], channel_multiplier=1).then_inc(ident_ready, 1)
            pool.wait_ge(ids_in, 16)
            pick_ids(0)
            for g in range(GRP):
                gather(M // GRP * g, M // GRP * (g + 1), gathered0[g])
            pool.wait_ge(w_summed, 2)
            half = M // 2
            nc.gpsimd.affine_select(out=w_extra[:, :, :], in_=w_ex[:, :].unsqueeze(1).broadcast_to([P, EXTRA, K]),
                                    compare_op=ALU.is_ge, fill=0.0, base=0,
                                    pattern=[[-half, EXTRA], [0, K]], channel_multiplier=1).then_inc(w_masked, 1)
            pool.wait_ge(w_masked, 1)
            nc.gpsimd.affine_select(out=w_extra[:, :, :], in_=w_extra[:, :, :],
                                    compare_op=ALU.is_ge, fill=0.0, base=half - 1,
                                    pattern=[[half, EXTRA], [0, K]], channel_multiplier=-1).then_inc(w_ready, 1)
            pool.wait_ge(emb_transposed, GRP)
            pick_ids(1)
            gather(0, GATHERED[1])
            body(0, False, False)
            with pool.Fori(1, TILES - 2) as t:
                body(t, False, False)
            body(TILES - 2, False, True)
            body(TILES - 1, True, True)

        @block.vector
        def _(dve):
            def product(t, s, k, in0, in1):
                if not (isinstance(t, int) and DVE_PH * phase(t, s) + DVE0 + k < Z_SLOTS):
                    dve.wait_ge(zd_used, dve_count(t, s, k + 1 - Z_SLOTS))
                nc.vector.tensor_tensor(z_dve[:, slot_dve(s, k), :, :], in0, in1, ALU.mult).then_inc(zd_made, 1)

            def cin_pair(t, s, layer, i, k):
                j = dve_pairs[i]
                s_in, v = x0b_ready(t, s, j)
                dve.wait_ge(s_in, v)
                if i == 0:
                    dve.wait_ge(xp_ready[layer], phase(t, s) + 1)
                product(t, s, k, xp[layer][:, :].unsqueeze(1).broadcast_to([P, 2, N]), x0b(s, j)[:, :, :])

            def layer0(t, s, k, block_no):
                dve.wait_ge(l0a_in, 3 * 16 * (block_no + 1))
                for i in range(CH0 // 2):
                    if i == 1:
                        dve.wait_ge(l0b_in, (CH0 - 2 + 2) * 16 * (block_no + 1))
                    product(t, s, k + i, x0_rep[:, :].unsqueeze(1).broadcast_to([P, 2, N]),
                            x0_rot[:, 2 * i:2 * i + 2, :])
                if not (isinstance(block_no, int) and block_no == 0):
                    dve.wait_ge(ze_used, block_no)
                nc.vector.tensor_tensor(z_extra[:, :], x0_lo[:, :], x0_hi[:, :], ALU.mult).then_inc(ze_made, 1)

            def reduce(t, s, which, n):
                part = (zpart, zsum)[s][which]
                rows = relu[which].shape[0]
                dve.wait_ge(relu_ready, n)
                if s == 1 and which == 0 and not (isinstance(t, int) and t == 0):
                    dve.wait_ge(h1_done, t)
                nc.vector.tensor_reduce(part[0:rows, :], relu[which][:, :].rearrange("p (d b) -> p b d", b=P),
                                        AXIS_X, ALU.add).then_inc(relu_reduced[which], 1)
                if s == 1:
                    dve.wait_ge(relu_reduced[which], phase(t, s) + 1)
                    nc.vector.tensor_tensor(part[0:rows, :], zpart[which][:, :], part[0:rows, :],
                                            ALU.add).then_inc(zsum_ready, 1)

            def body(t, first_tile, last_tile):
                for s in range(HALVES):
                    last = last_tile and s == 1
                    k = 0
                    for i in range(ND_P):
                        cin_pair(t, s, 0, i, k)
                        k += 1
                        if i == 3 and not (first_tile and s == 0):
                            pt, p_s = (t, 0) if s == 1 else (t - 1, 1)
                            reduce(pt, p_s, 1, sections(t, s, 0))
                    if not last:
                        layer0(t, s, k, phase(t, s) + 1)
                        k += CH0 // 2
                    for i in range(ND_P):
                        cin_pair(t, s, 1, i, k)
                        k += 1
                        if i == 1:
                            reduce(t, s, 0, sections(t, s, 1))

            dve.wait_ge(w0_in, 10 * 16)
            nc.vector.tensor_tensor(w_ex[:, :], w_ex[:, :], w_exb[:, :], ALU.add).then_inc(w_summed, 1)
            nc.vector.tensor_tensor(w_sym[:, :, :], w_sym[:, :, :], w_symb[:, :, :], ALU.add).then_inc(w_summed, 1)
            dve.wait_ge(w_summed, 2)
            nc.vector.tensor_scalar(w_sym[0:M, 0, :], w_sym[0:M, 0, :], 0.5, None, ALU.mult).then_inc(w_ready, 1)
            layer0(0, 0, -DVE0, 0)
            body(0, True, False)
            with dve.Fori(1, TILES - 1) as t:
                body(t, False, False)
            body(TILES - 1, False, True)
            reduce(TILES - 1, 1, 1, sections(TILES - 1, 1, 2))

        @block.scalar
        def _(act):
            def wait_l0(block_no):
                act.wait_ge(ze_used, block_no + 1)

            def wait_layer(t, s, k):
                act.wait_ge(zd_used, dve_count(t, s, k))

            def spread(t, s, layer, n, slot):
                for buf, ready in ((xp[layer], xp_ready[layer]), (xs[layer], xs_ready[layer])):
                    if not (isinstance(t, int) and phase(t, s) == 0):
                        pt, p_s = (t, 0) if s == 1 else (t - 1, 1)
                        if buf is xp[layer]:
                            k = ND_P if layer == 0 else DVE_PH
                            act.wait_ge(zd_made, dve_count(pt, p_s, k))
                        else:
                            act.wait_ge(zp_made, pool_count(pt, p_s, NP_P * (layer + 1)))
                    for copy in range(2):
                        for side in range(2):
                            ins = nc.scalar.activation(buf[K * copy:K * copy + K, NH * side:NH * side + NH],
                                                       acc[slot][K * side:K * side + K, :], ACT.Relu)
                    ins.then_inc(ready, 1)
                sum_input(t, s, layer, n, slot)

            def sum_input(t, s, layer, n, slot):
                which, row = layer // 2, layer % 2 * K
                if layer == 0 and not (isinstance(t, int) and phase(t, s) == 0):
                    act.wait_ge(relu_reduced[0], phase(t, s))
                if layer == 2 and not (isinstance(t, int) and phase(t, s) == 0):
                    act.wait_ge(relu_reduced[1], phase(t, s))
                for side in range(2):
                    ins = nc.scalar.activation(relu[which][row:row + K, NH * side:NH * side + NH],
                                               acc[slot][K * side:K * side + K, :], ACT.Relu)
                ins.then_inc(relu_ready, 1)

            def copy_x0(t, s, copies, copied):
                for j in copies:
                    s_in, v = x0b_in(t, s, j)
                    act.wait_ge(s_in, v)
                    for mi in range(2):
                        ins = nc.scalar.copy(x0b(s, j)[K * mi + K // 2:K * mi + K, :, :],
                                             x0b(s, j)[K * mi:K * mi + K // 2, :, :])
                    ins.then_inc(copied, 1)

            def write_x0t(t, g0, g1, written):
                for rep in range(2):
                    act.dma_start(bass.AP(x0t, t * (2 * M * ROW) + (rep * M * ROW + g0 * P * P),
                                          [[P, P], [P * P, g1 - g0], [1, P]]),
                                  emb_t[:, g0:g1, :]).then_inc(written, 16)

            def move_first_tile():
                for g in range(GRP):
                    act.wait_ge(emb_transposed, g + 1)
                    nc.scalar.copy(emb_t[:, g, :], ps_a[:, P * g:P * g + P]).then_inc(emb0_copied, 1)
                    act.wait_ge(emb0_copied, g + 1)
                    write_x0t(0, g, g + 1, x0t0_written[g])

            def move_tile(t):
                if isinstance(t, int) and t == 1:
                    for g in range(GRP):
                        act.wait_ge(x0t0_written[g], 32)
                else:
                    act.wait_ge(x0t_written, 32 * (t - 1))
                act.wait_ge(emb_transposed, GRP * (t + 1))
                nc.scalar.copy(emb_t[:, :, :], ps_a[:, :].rearrange("p (g b) -> p g b", g=GRP)).then_inc(emb_copied, 1)
                act.wait_ge(emb_copied, t)
                write_x0t(t, 0, GRP, x0t_written)

            def h1_out(t):
                act.wait_ge(h1_done, t + 1)
                for jc in range(JC1):
                    nc.scalar.activation(h1[:, jc, :], ps_a[:, P * jc:P * jc + P], ACT.Relu,
                                         bias=bt1_s[:, jc:jc + 1]).then_inc(h1_relu, 1)

            def h2_out(t):
                act.wait_ge(h2_done, t + 1)
                for jc in range(JC2):
                    ins = nc.scalar.activation(h2[:, jc, :], ps_b[:, P * jc:P * jc + P], ACT.Relu,
                                               bias=bt2_s[:, jc:jc + 1])
                ins.then_inc(h2_relu, 1)

            def y_out(t):
                act.wait_ge(y_done, t + 1)
                nc.scalar.copy(y_row[0:1, :], ps_b[0:1, 0:P]).then_inc(y_copied, 1)
                act.wait_ge(y_copied, t + 1)
                act.dma_start(bass.AP(out.tensor, t * P, [[P, 1], [1, P]]), y_row[0:1, :]).then_inc(out_written, 16)

            def body(t, first_tile, last_tile):
                for s in range(HALVES):
                    last = last_tile and s == 1
                    base = 3 * s
                    copy_x0(t, s, LATE_COPIES, late_copied)
                    wait_layer(t, s, ND_P)
                    spread(t, s, 1, sections(t, s, 1), (base + 1) % 2)
                    if s == 0 and not first_tile:
                        h1_out(t - 1)
                    if s == 1 and not first_tile and not last_tile:
                        y_out(t - 1)
                    if last:
                        h2_out(t - 1)
                    else:
                        nt, ns = (t, 1) if s == 0 else (t + 1, 0)
                        wait_l0(phase(t, s) + 1)
                        spread(nt, ns, 0, sections(t, s, 2), (base + 2) % 2)
                        copy_x0(nt, ns, EARLY_COPIES, early_copied)
                    n = sections(t, s, 3) if not last else sections(t, s, 2)
                    slot = (base + 3) % 2 if not last else (base + 2) % 2
                    wait_layer(t, s, after_l1(last) + ND_P)
                    sum_input(t, s, 2, n, slot)
                    if s == 0 and not first_tile and not last_tile:
                        h2_out(t - 1)
                    if s == 0 and not last_tile:
                        move_tile(t + 1)
                if last_tile:
                    y_out(t - 1)
                if not first_tile:
                    act.wait_ge(out_written, 16 * t)

            for rep in range(2):
                act.dma_start(bass.AP(w0h, rep * H * K, [[2 * H * K, M], [1, H * K]]),
                              w0.rearrange("m h k -> m (h k)")).then_inc(w0_copied, 16)
                act.dma_start(bass.AP(w0m, rep * M * H * K, [[H * K, M], [1, H * K]]),
                              w0.rearrange("m h k -> m (h k)")).then_inc(w0_copied, 16)
            act.wait_ge(w0_copied, 64)
            act.dma_start(w_ex[:, :], bass.AP(w0h, (M // 2) * K,
                                              [[0, EXTRA], [(2 * H + 1) * K, M // 2], [1, K]])).then_inc(w0_in, 16)
            act.dma_start(w_exb[:, :], bass.AP(w0m, (M // 2) * H * K,
                                               [[0, EXTRA], [(H + 1) * K, M // 2], [1, K]])).then_inc(w0_in, 16)
            for q in range(4):
                act.dma_start(w_sym[M * q:M * q + M, :, :],
                              bass.AP(w0h, q * K, [[(2 * H + 1) * K, M], [4 * K, CH0], [1, K]])).then_inc(w0_in, 16)
                act.dma_start(w_symb[M * q:M * q + M, :, :],
                              bass.AP(w0m, q * H * K, [[(H + 1) * K, M], [4 * H * K, CH0], [1, K]])
                              ).then_inc(w0_in, 16)
            act.dma_start(w_cin[0][:, :, :],
                          w1.rearrange("m h k -> (m h) k").rearrange("(c p) k -> p c k", p=P)).then_inc(w1_in, 16)
            act.dma_start(w_cin[1][:, :, :],
                          w2.rearrange("m h k -> (m h) k").rearrange("(c p) k -> p c k", p=P)).then_inc(w2_in, 16)
            act.dma_start(wt1_s[0][:, :], wt1[0:2 * K, :]).then_inc(mlp_in, 16)
            act.dma_start(wt1_s[1][:, :], wt1[2 * K:3 * K + DENSE, :]).then_inc(mlp_in, 16)
            act.dma_start(wt2_s[:, :, :], wt2.rearrange("(p c) j -> p c j", p=P)).then_inc(mlp_in, 16)
            act.dma_start(wt3_s[:, :], wt3.rearrange("(p c) o -> p (c o)", p=P)).then_inc(mlp_in, 16)
            act.dma_start(bt1_s[:, :], bt1.rearrange("(p c) -> p c", p=P)).then_inc(mlp_in, 16)
            act.dma_start(bt2_s[:, :], bt2.rearrange("(p c) -> p c", p=P)).then_inc(mlp_in, 16)
            move_first_tile()
            act.wait_ge(mlp_in, 6 * 16)
            copy_x0(0, 0, EARLY_COPIES, early_copied)
            wait_l0(0)
            spread(0, 0, 0, 1, 0)
            body(0, True, False)
            with act.Fori(1, TILES - 1) as t:
                body(t, False, False)
            body(TILES - 1, False, True)
            h1_out(TILES - 1)
            h2_out(TILES - 1)
            y_out(TILES - 1)

        @block.tensor
        def _(pe):
            def claim(n, slot):
                if not (isinstance(n, int) and n <= 2):
                    pe.wait_ge(relu_ready, n - 2)

            def pair(a, z, weights, chunk0, start, stop):
                for c in range(2):
                    for side in range(2):
                        ins = nc.tensor.matmul(a[K * side:K * side + K, :], weights[:, chunk0 + c, :],
                                               z[:, c, NH * side:NH * side + NH],
                                               start=start and c == 0, stop=stop and c == 1)
                return ins

            def layer0(t, s, k, n, slot, block_no):
                a = acc[slot]
                claim(n, slot)
                for i in range(CH0 // 2):
                    pe.wait_ge(zd_made, dve_count(t, s, k + i + 1))
                    pair(a, z_dve[:, slot_dve(s, k + i), :, :], w_sym, 2 * i, i == 0, False).then_inc(zd_used, 1)
                pe.wait_ge(ze_made, block_no + 1)
                for e in range(EXTRA // 2):
                    for side in range(2):
                        ins = nc.tensor.matmul(a[K * side:K * side + K, NE * e:NE * e + NE],
                                               w_extra[:, EXTRA // 2 * side + e, :], z_extra[:, :],
                                               start=False, stop=e == EXTRA // 2 - 1)
                ins.then_inc(ze_used, 1)

            def layer(t, s, l, k, n, slot):
                claim(n, slot)
                kd, kp = k, l * NP_P
                for j in range(PAIRS):
                    if j in POOL_PAIRS:
                        pe.wait_ge(zp_made, pool_count(t, s, kp + 1))
                        z, used = z_pool[:, kp % ZP_SLOTS, :, :], zp_used
                        kp += 1
                    else:
                        pe.wait_ge(zd_made, dve_count(t, s, kd + 1))
                        z, used = z_dve[:, slot_dve(s, kd), :, :], zd_used
                        kd += 1
                    ins = pair(acc[slot], z, w_cin[l], 2 * j, j == 0, j == PAIRS - 1)
                    ins.then_inc(used, 1)

            def transpose_tile(t):
                if isinstance(t, int) and t == 0:
                    for g in range(GRP):
                        pe.wait_ge(gathered0[g], 16 * M // GRP)
                        if g > 0:
                            pe.wait_ge(emb0_copied, g)
                        nc.tensor.transpose(ps_a[:, P * g:P * g + P], emb[:, P * g:P * g + P],
                                            ident[:, :]).then_inc(emb_transposed, 1)
                    return
                pe.wait_ge(gathered, 16 * M * t)
                for g in range(GRP):
                    nc.tensor.transpose(ps_a[:, P * g:P * g + P], emb[:, P * g:P * g + P],
                                        ident[:, :]).then_inc(emb_transposed, 1)

            def mlp1(t, emb_read):
                pe.wait_ge(zsum_ready, 2 * (t + 1))
                pe.wait_ge(dense_in, 16 * (t + 1))
                pe.wait_ge(emb_copied, emb_read)
                for jc in range(JC1):
                    for i in range(2):
                        ins = nc.tensor.matmul(ps_a[:, P * jc:P * jc + P], wt1_s[i][:, jc:F1:JC1], zsum[i][:, :],
                                               start=i == 0, stop=i == 1)
                ins.then_inc(h1_done, 1)

            def mlp2(t):
                for jc in range(JC2):
                    for c in range(JC1):
                        if jc == 0:
                            pe.wait_ge(h1_relu, JC1 * t + c + 1)
                        ins = nc.tensor.matmul(ps_b[:, P * jc:P * jc + P], wt2_s[:, c, jc:F2:JC2],
                                               h1[:, c, :], start=c == 0, stop=c == JC1 - 1)
                ins.then_inc(h2_done, 1)

            def mlp3(t):
                pe.wait_ge(h2_relu, t + 1)
                for c in range(JC2):
                    ins = nc.tensor.matmul(ps_b[0:1, 0:P], wt3_s[:, c:c + 1], h2[:, c, :],
                                           start=c == 0, stop=c == JC2 - 1)
                ins.then_inc(y_done, 1)

            def keep_warm(n):
                for _i in range(n):
                    nc.tensor.matmul(ps_a[:, :], ident[:, :], emb_t[:, :, :].rearrange("p g b -> p (g b)"),
                                     start=True, stop=True)

            def body(t, first_tile, last_tile):
                for s in range(HALVES):
                    last = last_tile and s == 1
                    base = 3 * s
                    layer(t, s, 0, 0, sections(t, s, 1), (base + 1) % 2)
                    if not first_tile:
                        if s == 0:
                            mlp1(t - 1, t)
                        elif last_tile:
                            mlp2(t - 1)
                            keep_warm(WARM_LAST_X)
                        else:
                            mlp3(t - 1)
                    k = ND_P
                    if not last:
                        layer0(t, s, k, sections(t, s, 2), (base + 2) % 2, phase(t, s) + 1)
                        k += CH0 // 2
                    n = sections(t, s, 3) if not last else sections(t, s, 2)
                    layer(t, s, 1, k, n, (base + 3) % 2 if not last else (base + 2) % 2)
                    if s == 0 and not first_tile and not last_tile:
                        mlp2(t - 1)
                    if s == 0 and not last_tile:
                        transpose_tile(t + 1)
                if last_tile:
                    mlp3(t - 1)
                    keep_warm(WARM_LAST_Z)
                elif not first_tile:
                    pe.wait_ge(y_copied, t)

            pe.wait_ge(ident_ready, 1)
            transpose_tile(0)
            pe.wait_ge(emb0_copied, GRP)
            pe.wait_ge(x0t0_written[GRP - 1], 32)
            keep_warm(WARM_L0)
            pe.wait_ge(w_ready, 2)
            layer0(0, 0, -DVE0, 1, 0, 0)
            keep_warm(WARM_FIRST_X)
            pe.wait_ge(w1_in, 16)
            pe.wait_ge(w2_in, 16)
            pe.wait_ge(mlp_in, 6 * 16)
            body(0, True, False)
            with pe.Fori(1, TILES - 1) as t:
                body(t, False, False)
            body(TILES - 1, False, True)
            mlp1(TILES - 1, TILES - 1)
            pe.wait_ge(y_copied, TILES - 1)
            mlp2(TILES - 1)
            mlp3(TILES - 1)


N_TABLES = 32


def kernel(**inputs):
    import numpy as _np
    import concourse.bacc as _bacc
    from concourse import mybir as _mybir
    from concourse.bass_utils import run_bass_kernel_spmd as _run

    nc = _bacc.Bacc("TRN2", target_bir_lowering=False, num_devices=1)
    arrays = {}

    def dram(name, transposed=False):
        a = _np.ascontiguousarray(_np.asarray(inputs[name]).T if transposed else inputs[name])
        arrays[f"in_{name}_dram"] = a
        return nc.dram_tensor(f"in_{name}_dram", a.shape, _mybir.dt.from_np(a.dtype), kind="ExternalInput").ap()

    tables = [dram(f"tbl_{f}") for f in range(N_TABLES)]
    out = nc.dram_tensor("out_0_dram", (inputs["ids"].shape[0], 1), F32, kind="ExternalOutput").ap()
    cin_tower(nc, dram("dense_ctx", transposed=True), dram("ids"), tables, dram("L0_rec_W0"), dram("L0_rec_W1"), dram("L0_rec_W2"),
              dram("W_top1"), dram("b_top1"), dram("W_top2"), dram("b_top2"), dram("W_top3"), out)
    r = _run(nc, [arrays], core_ids=[0])
    return r.results[0]["out_0_dram"]
```
